# Optimizing a Trainium2 kernel written in Bass

```python
import numpy as np
import jax
import jax.numpy as jnp

def _softmax(x, axis=-1):
    return jax.nn.softmax(x, axis=axis)

def _gelu(x):
    return jax.nn.gelu(x, approximate=True)

def _silu(x):
    return jax.nn.silu(x)

def _sigmoid(x):
    return jax.nn.sigmoid(x)

def _layernorm(x, axis=-1, eps=1e-05):
    m = jnp.mean(x, axis=axis, keepdims=True)
    v = jnp.var(x, axis=axis, keepdims=True)
    return (x - m) / jnp.sqrt(v + eps)

def _scatter_add(tgt, idx, src, axis=0):
    return tgt.at[idx].add(src)

def _segment_sum(src, seg, n):
    return jax.ops.segment_sum(src, seg, n)
kernel_name = 'mk_cond_resid_d1_seqx_r2_0a40cd'

def setup_inputs(seed: int=0):
    np.random.seed(seed)
    _w = jnp.asarray

    def _rec_inputs():
        import jax
        import jax.numpy as jnp
        _rk = jax.random.key(seed)
        x = -0.000125 + 0.9999 * jax.random.normal(jax.random.fold_in(_rk, 1), (8, 512, 512), jnp.float32)
        _lenS = 512 - jax.random.randint(jax.random.fold_in(_rk, 7), (8,), 0, max(1, 512 // 4) + 1, jnp.int32)
        _lenS2 = 512 - jax.random.randint(jax.random.fold_in(_rk, 8), (8,), 0, max(1, 512 // 4) + 1, jnp.int32)
        cond_1024 = -0.00493535 + 1.00056 * jax.random.normal(jax.random.fold_in(_rk, 11), (8, 512), jnp.float32)
        return (x, cond_1024)
    x, cond_1024 = _rec_inputs()

    def _L0_cond_setup():
        import jax, jax.numpy as jnp
        import numpy as np
        INPUT_DIM = 512
        LATENT_DIM = 512
        key = jax.random.key(seed)
        ks = jax.random.split(key, 8)
        B, T = (64, 256)
        concat_dim = INPUT_DIM + LATENT_DIM
        s = lambda fan_in: 1.0 / np.sqrt(fan_in)
        return {'x': jax.random.normal(ks[0], (B, T, INPUT_DIM), dtype=jnp.float32), 'h0': jax.random.normal(ks[1], (B, LATENT_DIM), dtype=jnp.float32), 'w_W': jax.random.uniform(ks[2], (concat_dim, 2 * LATENT_DIM), jnp.float32, -s(concat_dim), s(concat_dim)), 'w_b': jax.random.uniform(ks[3], (2 * LATENT_DIM,), jnp.float32, -s(concat_dim), s(concat_dim)), 'wx_W': jax.random.uniform(ks[4], (INPUT_DIM, LATENT_DIM), jnp.float32, -s(INPUT_DIM), s(INPUT_DIM)), 'wx_b': jax.random.uniform(ks[5], (LATENT_DIM,), jnp.float32, -s(INPUT_DIM), s(INPUT_DIM)), 'wh_W': jax.random.uniform(ks[6], (LATENT_DIM, LATENT_DIM), jnp.float32, -s(LATENT_DIM), s(LATENT_DIM)), 'wh_b': jax.random.uniform(ks[7], (LATENT_DIM,), jnp.float32, -s(LATENT_DIM), s(LATENT_DIM))}
    _L0_cond_all = _L0_cond_setup()
    _L0_cond_in = {k: v for k, v in _L0_cond_all.items() if k in ('w_W', 'w_b', 'wx_W', 'wx_b', 'wh_W', 'wh_b')}
    del _L0_cond_all
    return {'x': x, 'cond_1024': cond_1024, 'L0_cond_w_W': _L0_cond_in['w_W'], 'L0_cond_w_b': _L0_cond_in['w_b'], 'L0_cond_wx_W': _L0_cond_in['wx_W'], 'L0_cond_wx_b': _L0_cond_in['wx_b'], 'L0_cond_wh_W': _L0_cond_in['wh_W'], 'L0_cond_wh_b': _L0_cond_in['wh_b']}

def reference(x, cond_1024, L0_cond_w_W, L0_cond_w_b, L0_cond_wx_W, L0_cond_wx_b, L0_cond_wh_W, L0_cond_wh_b):
    import jax
    import jax.numpy as jnp

    def _L0_cond_ref(x, h0, w_W, w_b, wx_W, wx_b, wh_W, wh_b):
        import jax, jax.numpy as jnp
        import numpy as np
        INPUT_DIM = 512
        LATENT_DIM = 512
        xT = jnp.swapaxes(x, 0, 1)

        def step(h, x_t):
            fused = jax.nn.sigmoid(jnp.concatenate([x_t, h], axis=-1) @ w_W + w_b)
            hidden_state, output_state = jnp.split(fused, 2, axis=-1)
            memory_state = x_t @ wx_W + wx_b + hidden_state * (h @ wh_W + wh_b)
            h_new = output_state * h + (1.0 - output_state) * jnp.tanh(memory_state)
            return (h_new, h_new)
        _, hs = jax.lax.scan(step, h0, xT)
        return jnp.swapaxes(hs, 0, 1)
    x = x + _L0_cond_ref(x, cond_1024, L0_cond_w_W, L0_cond_w_b, L0_cond_wx_W, L0_cond_wx_b, L0_cond_wh_W, L0_cond_wh_b)
    return x

_drawn_inputs = setup_inputs


def setup_inputs(seed=0):
    import zlib

    import numpy as np

    out = dict(_drawn_inputs(seed))
    spreads = {}
    factors = {'L0_cond_w_b': 25.789, 'L0_cond_wx_b': 2.765, 'L0_cond_wh_b': 5.617}
    for name, (base, spread) in spreads.items():
        noise = np.random.default_rng([zlib.crc32(name.encode()), seed]).standard_normal(out[name].shape)
        drawn = base * np.exp(spread * noise) if base else spread * noise
        out[name] = jnp.asarray(drawn.astype(out[name].dtype))
    for name, factor in factors.items():
        out[name] = (out[name] * factor).astype(out[name].dtype)
    return out
```

```python
import concourse.bass as bass
from concourse import mybir
from contextlib import ExitStack

F32 = mybir.dt.float32
BF16 = mybir.dt.bfloat16
ALU = mybir.AluOpType
ACT = mybir.ActivationFunctionType
AX = mybir.AxisListType

P = 128


def build(nc, x, h0, w_W, w_b, wx_W, wx_b, wh_W, wh_b, out):
    KC, T, B = x.shape[1], x.shape[2], x.shape[3]
    D = KC * P
    GATES = 3
    R, Z, M = range(GATES)
    N = GATES * D
    PARTS = 3
    HALVES = 2
    HC = KC // HALVES
    HB = HC * B
    STEPS = 16
    BLOCKS = T // STEPS
    TOK = STEPS * B
    SLOTS = PARTS + 1
    UNITS = GATES * KC
    Y_HALF = STEPS // 2

    x_list = [(u, k) for u in range(UNITS) for k in range(KC)]
    x_cut = [-(-len(x_list) * s // (STEPS - 1)) for s in range(STEPS)] + [len(x_list)]
    X_PLAN = [x_list[x_cut[s]:x_cut[s + 1]] for s in range(STEPS)]
    X_ENDS = [[u for u, k in plan if k == KC - 1] for plan in X_PLAN]
    assert not X_PLAN[STEPS - 1]

    ctx = ExitStack()
    with ctx:
        def sb(name, shape, dt):
            return ctx.enter_context(nc.sbuf_tensor(name, shape, dt))

        def sem(name):
            return ctx.enter_context(nc.semaphore(name))

        def halves(name):
            return [sem(f"{name}{o}") for o in range(HALVES)]

        x_sb = sb("x_sb", [P, KC, T * B], F32)
        wx = sb("wx", [P, KC, N], F32)
        wh_rest = sb("wh_rest", [P, KC, N], F32)
        wh = sb("wh", [P, PARTS, KC, N], BF16)
        bias_x = sb("bias_x", [P, UNITS], F32)
        bias_h = sb("bias_h", [P, KC], F32)
        xg = sb("xg", [P, 2, STEPS, GATES, HALVES, HB], F32)
        h = sb("h", [P, PARTS, STEPS, KC, B], F32)
        y = sb("y", [P, KC, STEPS, B], F32)
        pre = sb("pre", [P, HALVES, 2, HB], F32)
        r_gate = sb("r_gate", [P, HALVES, HB], F32)
        z_gate = sb("z_gate", [P, HALVES, HB], F32)
        one_minus_z = sb("one_minus_z", [P, HALVES, HB], F32)
        zh = sb("zh", [P, HALVES, HB], F32)
        m_terms = sb("m_terms", [P, HALVES, HC, SLOTS + 1, B], F32)
        m_pre = sb("m_pre", [P, HALVES, HB], F32)
        n_tanh = sb("n_tanh", [P, HALVES, HB], F32)
        zn = sb("zn", [P, HALVES, HB], F32)

        ps = ctx.enter_context(nc.psum_tensor("ps", [P, 8, 512], F32))
        X_BANK = GATES * HALVES

        def bank(o, g):
            return GATES * o + g

        def slots(o, g):
            return ps[:, bank(o, g), 0:HC * SLOTS * B].rearrange("p (c s b) -> p c s b", c=HC, s=SLOTS)

        def top_halves(part, step, k):
            return h[:, part, step, k, :].bitcast(BF16)

        h_bf = h[:, :, :, :, :].bitcast(BF16)

        def h_half(part, s, o):
            return h[:, part, s, HC * o:HC * (o + 1), :]

        def h_half_top(part, s, o):
            return h_bf[:, part, s, HC * o:HC * (o + 1), 1::2]

        def cb(ap):
            return ap.rearrange("p (c b) -> p c b", c=HC)

        bias_loaded = sem("bias_loaded")
        h0_loaded = sem("h0_loaded")
        wh_loaded = [sem(f"wh_loaded{k}") for k in range(KC)]
        wx_loaded = sem("wx_loaded")
        x_loaded = sem("x_loaded")
        y_stored = sem("y_stored")
        part_cut = [sem(f"part_cut{k}") for k in range(KC)]
        rest_left = [sem(f"rest_left{k}") for k in range(KC)]
        start_rest = sem("start_rest")
        product = [[sem(f"product{o}{g}") for g in range(GATES)] for o in range(HALVES)]
        x_product = sem("x_product")
        pre_ready = [[sem(f"pre_ready{o}{g}") for g in (R, Z)] for o in range(HALVES)]
        m_scaled = halves("m_scaled")
        m_pre_ready = halves("m_pre_ready")
        zn_ready = halves("zn_ready")
        h_written = halves("h_written")
        rest1_written = halves("rest1_written")
        h_ready = halves("h_ready")
        r_ready = halves("r_ready")
        z_ready = halves("z_ready")
        omz_ready = halves("omz_ready")
        tanh_ready = halves("tanh_ready")
        refilled = halves("refilled")
        cm_placed = sem("cm_placed")
        xg_ready = sem("xg_ready")
        zh_ready = halves("zh_ready")
        xm_placed = halves("xm_placed")
        y_early = sem("y_early")
        y_late = sem("y_late")

        block = ctx.enter_context(nc.Block())

        def held(eng, value):
            return value if isinstance(value, int) else eng.snap(value)

        @block.sync
        def _(sp):
            sp.sem_inc(y_stored, 16)
            sp.dma_start(h[:, 0, STEPS - 1, :, :], h0).then_inc(h0_loaded, 16)
            sp.dma_start(bias_x[:, 0:2 * KC], w_b).then_inc(bias_loaded, 16)
            sp.dma_start(bias_x[:, 2 * KC:3 * KC], wx_b).then_inc(bias_loaded, 16)
            sp.dma_start(bias_h[:, :], wh_b).then_inc(bias_loaded, 16)
            for k in range(KC):
                sp.dma_start(wh_rest[:, k, 0:2 * D], w_W[D + k * P:D + (k + 1) * P, :]).then_inc(wh_loaded[k], 16)
                sp.dma_start(wh_rest[:, k, 2 * D:N], wh_W[k * P:(k + 1) * P, :]).then_inc(wh_loaded[k], 16)
            x_flat = x.rearrange("p c t b -> p c (t b)")
            out_flat = out.rearrange("p c t b -> p c (t b)")
            sp.dma_start(x_sb[:, :, 0:TOK], x_flat[:, :, 0:TOK]).then_inc(x_loaded, 16)
            for k in range(KC):
                sp.dma_start(wx[:, k, 0:2 * D], w_W[k * P:(k + 1) * P, :]).then_inc(wx_loaded, 16)
                sp.dma_start(wx[:, k, 2 * D:N], wx_W[k * P:(k + 1) * P, :]).then_inc(wx_loaded, 16)
            with sp.Fori(1, BLOCKS) as i:
                sp.wait_ge(x_loaded, sp.snap(i * 16))
                cols = bass.ds(sp.snap(i * TOK), TOK)
                sp.dma_start(x_sb[:, :, cols], x_flat[:, :, cols]).then_inc(x_loaded, 16)
            with sp.Fori(0, BLOCKS) as i:
                done = sp.snap(i + 2)
                sp.wait_ge(y_early, done)
                sp.wait_ge(y_late, done)
                sp.dma_start(out_flat[:, :, bass.ds(sp.snap(i * TOK), TOK)],
                             y[:, :, :, :].rearrange("p c t b -> p c (t b)")).then_inc(y_stored, 16)
            sp.wait_ge(y_stored, 16 * (BLOCKS + 1))

        @block.tensor
        def _(pe):
            def x_products(plan, i_next, unit0):
                for u, k in plan:
                    g, c = divmod(u, KC)
                    if k == 0 and not (isinstance(unit0, int) and unit0 + u < 2):
                        pe.wait_ge(xg_ready, unit0 + (u - 1))
                    cols = slice(0, TOK) if isinstance(i_next, int) and i_next == 0 else bass.ds(i_next * TOK, TOK)
                    mm = pe.matmul(ps[:, X_BANK + u % 2, 0:TOK], wx[:, k, g * D + c * P:g * D + (c + 1) * P],
                                   x_sb[:, k, cols], start=(k == 0), stop=(k == KC - 1))
                    if k == KC - 1:
                        mm.then_inc(x_product, 1)

            def products(o, g, chunks, ks, s):
                for ci in chunks:
                    col = g * D + (HC * o + ci) * P
                    for k in ks:
                        for part in range(PARTS):
                            mm = pe.matmul(ps[:, bank(o, g), ci * SLOTS * B:(ci * SLOTS + PARTS) * B],
                                           wh[:, part, k, col:col + P], h_bf[:, :, s - 1 if s else STEPS - 1, k, 1::2],
                                           start=(ci == 0 and k == 0 and part == 0),
                                           stop=(ci == HC - 1 and k == KC - 1 and part == PARTS - 1),
                                           skip_group_check=True)
                return mm

            ALL, FIRST, SECOND = range(HC), range(HC), range(HC, KC)

            def step(t0, s):
                nxt = held(pe, t0 + (s + 1))
                pe.wait_ge(h_ready[0], nxt)
                pe.wait_ge(refilled[0], nxt)
                products(0, R, ALL, FIRST, s)
                products(0, Z, ALL, FIRST, s)
                products(0, M, ALL, FIRST, s)
                pe.wait_ge(refilled[1], nxt)
                products(1, R, ALL, FIRST, s)
                products(1, Z, range(1), FIRST, s)
                pe.wait_ge(h_ready[1], nxt)
                for g in range(GATES):
                    products(0, g, ALL, SECOND, s).then_inc(product[0][g], 1)
                products(1, Z, range(1, HC), FIRST, s)
                products(1, M, ALL, FIRST, s)
                for g in range(GATES):
                    products(1, g, ALL, SECOND, s).then_inc(product[1][g], 1)

            pe.wait_ge(x_loaded, 16)
            pe.wait_ge(wx_loaded, 2 * KC * 16)
            x_products(x_list, 0, 0)
            for k in range(KC):
                pe.wait_ge(part_cut[k], PARTS)
            pe.wait_ge(cm_placed, 1)
            with pe.Fori(0, BLOCKS - 1) as i:
                t0 = pe.snap(i * STEPS)
                nxt_block = pe.snap(i + 1)
                unit0 = pe.snap(i * UNITS + UNITS)
                pe.wait_ge(x_loaded, pe.snap(t0 + 2 * 16))
                for s in range(STEPS):
                    step(t0, s)
                    x_products(X_PLAN[s], nxt_block, unit0)
            for s in range(STEPS):
                step(STEPS * (BLOCKS - 1), s)

        @block.scalar
        def _(act):
            def refill(o, s, which):
                src = xg[:, which, s, R:Z + 1, o, :].rearrange("p a g (c b) -> p (a g) c b", c=HC)
                dst = ps[:, bank(o, R):bank(o, Z) + 1, 0:HC * SLOTS * B] \
                    .rearrange("p g (c s b) -> p g c s b", c=HC, s=SLOTS)[:, :, :, PARTS, :]
                act.activation(dst, src, ACT.Copy).then_inc(refilled[o], 1)

            def empty(u, which, unit0):
                g, c = divmod(u, KC)
                o, ci = divmod(c, HC)
                act.wait_ge(x_product, unit0 + (u + 1))
                act.wait_ge(bias_loaded, 3 * 16)
                dst = xg[:, which, :, g, o, ci * B:(ci + 1) * B].rearrange("p a t b -> p (a t) b")
                act.activation(dst, ps[:, X_BANK + u % 2, 0:TOK].rearrange("p (t b) -> p t b", b=B),
                               ACT.Identity, bias=bias_x[:, u:u + 1]).then_inc(xg_ready, 1)

            def step(t0, s, this, other, unit0, last):
                nxt = held(act, t0 + (s + 1))
                if not last and s:
                    for u in X_ENDS[s - 1]:
                        empty(u, other, unit0)
                for o in range(HALVES):
                    act.wait_ge(pre_ready[o][R], nxt)
                    act.activation(r_gate[:, o, :], pre[:, o, R, :], ACT.Sigmoid).then_inc(r_ready[o], 1)
                    act.wait_ge(pre_ready[o][Z], nxt)
                    act.activation(z_gate[:, o, :], pre[:, o, Z, :], ACT.Sigmoid).then_inc(z_ready[o], 1)
                    act.activation(one_minus_z[:, o, :], pre[:, o, Z, :], ACT.Sigmoid, scale=-1.0)\
                        .then_inc(omz_ready[o], 1)
                    if s == STEPS - 1 and o == 0 and not last:
                        act.wait_ge(xg_ready, unit0 + UNITS)
                    act.wait_ge(m_pre_ready[o], nxt)
                    act.activation(n_tanh[:, o, :], m_pre[:, o, :], ACT.Tanh).then_inc(tanh_ready[o], 1)
                    if s < STEPS - 1:
                        refill(o, s + 1, this)
                    elif not last:
                        refill(o, 0, other)

            act.wait_ge(bias_loaded, 3 * 16)
            act.activation(n_tanh[:, 0, 0:KC], bias_h[:, :], ACT.Sigmoid)
            for part in range(PARTS):
                for k in range(KC):
                    if part == 0:
                        act.wait_ge(wh_loaded[k], 2 * 16)
                    else:
                        act.wait_ge(rest_left[k], part)
                    act.activation(wh[:, part, k, :], wh_rest[:, k, :], ACT.Copy).then_inc(part_cut[k], 1)
            for o in range(HALVES):
                cm = bias_h[:, HC * o:HC * (o + 1)].unsqueeze(2).to_broadcast([P, HC, B])
                last_cm = act.activation(slots(o, M)[:, :, PARTS, :], cm, ACT.Copy)
            last_cm.then_inc(cm_placed, 1)
            for u in range(UNITS):
                empty(u, slice(0, 1), 0)
            act.wait_ge(xg_ready, UNITS)
            for o in range(HALVES):
                refill(o, 0, slice(0, 1))
            with act.Fori(0, BLOCKS - 1) as i:
                t0 = act.snap(i * STEPS)
                this = bass.ds(act.snap(i % 2), 1)
                other = bass.ds(act.snap((i + 1) % 2), 1)
                unit0 = act.snap(i * UNITS + UNITS)
                for s in range(STEPS):
                    step(t0, s, this, other, unit0, False)
            final = slice((BLOCKS - 1) % 2, (BLOCKS - 1) % 2 + 1)
            for s in range(STEPS):
                step(STEPS * (BLOCKS - 1), s, final, None, None, True)

        @block.vector
        def _(dve):
            def gate_sum(o, g, nxt):
                dve.wait_ge(product[o][g], nxt)
                dve.tensor_reduce(cb(pre[:, o, g, :]), slots(o, g).rearrange("p c s b -> p c b s"),
                                  AX.X, ALU.add).then_inc(pre_ready[o][g], 1)

            def m_scale(o, nxt):
                dve.wait_ge(product[o][M], nxt)
                dve.wait_ge(r_ready[o], nxt)
                r = cb(r_gate[:, o, :]).unsqueeze(2).to_broadcast([P, HC, SLOTS, B])
                dve.tensor_tensor(m_terms[:, o, :, 0:SLOTS, :], slots(o, M), r, ALU.mult).then_inc(m_scaled[o], 1)

            def m_sum(o, nxt):
                dve.wait_ge(m_scaled[o], nxt)
                dve.wait_ge(xm_placed[o], nxt)
                dve.tensor_reduce(cb(m_pre[:, o, :]), m_terms[:, o, :, :, :].rearrange("p c s b -> p c b s"),
                                  AX.X, ALU.add).then_inc(m_pre_ready[o], 1)

            def scale_n(o, nxt):
                dve.wait_ge(omz_ready[o], nxt)
                dve.wait_ge(tanh_ready[o], nxt)
                dve.tensor_tensor(zn[:, o, :], one_minus_z[:, o, :], n_tanh[:, o, :], ALU.mult)\
                    .then_inc(zn_ready[o], 1)

            def write_h(o, s, nxt):
                dve.wait_ge(zn_ready[o], nxt)
                dve.wait_ge(zh_ready[o], nxt)
                dve.tensor_tensor(h_half(0, s, o), cb(zn[:, o, :]), cb(zh[:, o, :]), ALU.add)\
                    .then_inc(h_written[o], 1)

            def write_rest1(o, s, nxt):
                dve.wait_ge(h_written[o], nxt)
                dve.tensor_tensor(h_half(1, s, o), h_half(0, s, o), h_half_top(0, s, o), ALU.subtract)\
                    .then_inc(rest1_written[o], 1)

            def write_rest2(o, s, nxt):
                dve.wait_ge(rest1_written[o], nxt)
                dve.tensor_tensor(h_half(2, s, o), h_half(1, s, o), h_half_top(1, s, o), ALU.subtract)\
                    .then_inc(h_ready[o], 1)

            def step(t0, i, s):
                nxt = held(dve, t0 + (s + 1))
                if s == 0:
                    dve.wait_ge(y_early, held(dve, i + 1))
                if s == Y_HALF:
                    dve.wait_ge(y_late, held(dve, i + 1))
                gate_sum(0, R, nxt)
                gate_sum(0, Z, nxt)
                m_scale(0, nxt)
                m_sum(0, nxt)
                scale_n(0, nxt)
                gate_sum(1, R, nxt)
                write_h(0, s, nxt)
                gate_sum(1, Z, nxt)
                write_rest1(0, s, nxt)
                write_rest2(0, s, nxt)
                m_scale(1, nxt)
                m_sum(1, nxt)
                scale_n(1, nxt)
                write_h(1, s, nxt)
                write_rest1(1, s, nxt)
                write_rest2(1, s, nxt)

            S = STEPS - 1
            dve.wait_ge(h0_loaded, 16)
            for o in range(HALVES):
                dve.tensor_tensor(h_half(1, S, o), h_half(0, S, o), h_half_top(0, S, o), ALU.subtract)\
                    .then_inc(start_rest, 1)
            for o in range(HALVES):
                dve.wait_ge(start_rest, o + 1)
                dve.tensor_tensor(h_half(2, S, o), h_half(1, S, o), h_half_top(1, S, o), ALU.subtract)\
                    .then_inc(h_ready[o], 1)
            for part in range(PARTS - 1):
                for k in range(KC):
                    dve.wait_ge(part_cut[k], part + 1)
                    dve.tensor_tensor(wh_rest[:, k, :], wh_rest[:, k, :], wh[:, part, k, :], ALU.subtract)\
                        .then_inc(rest_left[k], 1)
            with dve.Fori(0, BLOCKS - 1) as i:
                t0 = dve.snap(i * STEPS)
                for s in range(STEPS):
                    step(t0, i, s)
            for s in range(STEPS):
                step(STEPS * (BLOCKS - 1), BLOCKS - 1, s)

        @block.gpsimd
        def _(pool):
            def place_xm(o, s, which):
                pool.tensor_copy(m_terms[:, o, :, SLOTS, :],
                                 xg[:, which, s, M, o, :].rearrange("p a (c b) -> p (a c) b", c=HC))\
                    .then_inc(xm_placed[o], 1)

            def add_x(s0, base, early_or_late):
                cols = base + s0 * B
                xs = x_sb[:, :, cols:cols + Y_HALF * B] if isinstance(cols, int) else \
                    x_sb[:, :, bass.ds(cols, Y_HALF * B)]
                pool.tensor_tensor(y[:, :, s0:s0 + Y_HALF, :],
                                   xs.rearrange("p c (t b) -> p c t b", b=B),
                                   h[:, 0, s0:s0 + Y_HALF, :, :].rearrange("p t c b -> p c t b"), ALU.add)\
                    .then_inc(early_or_late, 1)

            def step(t0, i, s, this, other, unit0, last):
                nxt = held(pool, t0 + (s + 1))
                for o in range(HALVES):
                    if not last or s < STEPS - 1:
                        if s == STEPS - 1 and o == 0:
                            pool.wait_ge(xg_ready, unit0 + UNITS)
                    pool.wait_ge(z_ready[o], nxt)
                    pool.tensor_tensor(cb(zh[:, o, :]), cb(z_gate[:, o, :]), h_half(0, s - 1 if s else STEPS - 1, o),
                                       ALU.mult).then_inc(zh_ready[o], 1)
                    if not last or s < STEPS - 1:
                        pool.wait_ge(m_pre_ready[o], nxt)
                        pool.wait_ge(xg_ready, UNITS)
                        place_xm(o, (s + 1) % STEPS, this if s < STEPS - 1 else other)
                if s % Y_HALF == Y_HALF - 1:
                    pool.wait_ge(h_written[0], nxt)
                    pool.wait_ge(h_written[1], nxt)
                    if s == Y_HALF - 1:
                        pool.wait_ge(y_stored, held(pool, t0 + 16))
                    pool.wait_ge(x_loaded, 16)
                    add_x(s + 1 - Y_HALF, t0 * B, y_early if s < Y_HALF else y_late)

            pool.sem_inc(y_early, 1)
            pool.sem_inc(y_late, 1)
            pool.wait_ge(xg_ready, UNITS)
            for o in range(HALVES):
                place_xm(o, 0, slice(0, 1))
            with pool.Fori(0, BLOCKS - 1) as i:
                t0 = pool.snap(i * STEPS)
                this = bass.ds(pool.snap(i % 2), 1)
                other = bass.ds(pool.snap((i + 1) % 2), 1)
                unit0 = pool.snap(i * UNITS + UNITS)
                for s in range(STEPS):
                    step(t0, i, s, this, other, unit0, False)
            final = slice((BLOCKS - 1) % 2, (BLOCKS - 1) % 2 + 1)
            for s in range(STEPS):
                step(STEPS * (BLOCKS - 1), BLOCKS - 1, s, final, None, None, True)


def kernel(x, cond_1024, L0_cond_w_W, L0_cond_w_b, L0_cond_wx_W, L0_cond_wx_b, L0_cond_wh_W, L0_cond_wh_b):
    import numpy as np
    import concourse.bacc as bacc
    from concourse.bass_utils import run_bass_kernel_spmd

    x, cond = np.asarray(x), np.asarray(cond_1024)
    B, T, D = x.shape
    KC = D // P

    def columns(v):
        return np.ascontiguousarray(np.asarray(v).reshape(-1, P).transpose(1, 0))

    arrays = {
        "x": np.ascontiguousarray(x.reshape(B, T, KC, P).transpose(3, 2, 1, 0)),
        "h0": np.ascontiguousarray(cond.reshape(B, KC, P).transpose(2, 1, 0)),
        "w_W": np.ascontiguousarray(L0_cond_w_W),
        "w_b": columns(L0_cond_w_b),
        "wx_W": np.ascontiguousarray(L0_cond_wx_W),
        "wx_b": columns(L0_cond_wx_b),
        "wh_W": np.ascontiguousarray(L0_cond_wh_W),
        "wh_b": columns(L0_cond_wh_b),
    }
    nc = bacc.Bacc("TRN2", target_bir_lowering=False, num_devices=1)
    args = {n: nc.dram_tensor(f"in_{n}", a.shape, F32, kind="ExternalInput").ap() for n, a in arrays.items()}
    out = nc.dram_tensor("out_h", (P, KC, T, B), F32, kind="ExternalOutput").ap()
    build(nc, out=out, **args)
    r = run_bass_kernel_spmd(nc, [{f"in_{n}": a for n, a in arrays.items()}], core_ids=[0])
    got = r.results[0]["out_h"]
    return np.ascontiguousarray(got.transpose(3, 2, 1, 0).reshape(B, T, D))
```

```python
import concourse.bass as bass
from concourse import mybir
from contextlib import ExitStack

F32 = mybir.dt.float32
BF16 = mybir.dt.bfloat16
ALU = mybir.AluOpType
ACT = mybir.ActivationFunctionType
AX = mybir.AxisListType

P = 128


def build(nc, x, h0, w_W, w_b, wx_W, wx_b, wh_W, wh_b, out):
    KC, T, B = x.shape[1], x.shape[2], x.shape[3]
    D = KC * P
    GATES = 3
    R, Z, M = range(GATES)
    N = GATES * D
    PARTS = 3
    HALVES = 2
    HC = KC // HALVES
    HB = HC * B
    STEPS = 16
    BLOCKS = T // STEPS
    TOK = STEPS * B
    SLOTS = PARTS + 1
    UNITS = GATES * KC
    Y_HALF = STEPS // 2

    x_list = [(u, k) for u in range(UNITS) for k in range(KC)]
    X_PER_STEP = len(x_list) // STEPS
    X_PLAN = [x_list[X_PER_STEP * s:X_PER_STEP * (s + 1)] for s in range(STEPS)]
    X_ENDS = [[u for u, k in plan if k == KC - 1] for plan in X_PLAN]
    assert X_ENDS[STEPS - 1] == [UNITS - 1]

    ctx = ExitStack()
    with ctx:
        def sb(name, shape, dt):
            return ctx.enter_context(nc.sbuf_tensor(name, shape, dt))

        def sem(name):
            return ctx.enter_context(nc.semaphore(name))

        def halves(name):
            return [sem(f"{name}{o}") for o in range(HALVES)]

        x_sb = sb("x_sb", [P, KC, T * B + B], F32)
        wx = sb("wx", [P, KC, N], F32)
        wh_rest = sb("wh_rest", [P, KC, N], F32)
        wh = sb("wh", [P, PARTS, KC, N], BF16)
        bias_x = sb("bias_x", [P, UNITS], F32)
        bias_h = sb("bias_h", [P, KC], F32)
        xg = sb("xg", [P, 2, STEPS, GATES, HALVES, HB], F32)
        xg_0 = sb("xg_0", [P, 1, 1, GATES, HALVES, HB], F32)
        h = sb("h", [P, PARTS, STEPS, KC, B], F32)
        y = sb("y", [P, KC, STEPS, B], F32)
        pre = sb("pre", [P, HALVES, 2, HB], F32)
        r_gate = sb("r_gate", [P, HALVES, HB], F32)
        z_gate = sb("z_gate", [P, HALVES, HB], F32)
        one_minus_z = sb("one_minus_z", [P, HALVES, HB], F32)
        zh = sb("zh", [P, HALVES, HB], F32)
        m_terms = sb("m_terms", [P, HALVES, HC, SLOTS + 1, B], F32)
        m_pre = sb("m_pre", [P, HALVES, HB], F32)
        n_tanh = sb("n_tanh", [P, HALVES, HB], F32)
        zn = sb("zn", [P, HALVES, HB], F32)

        ps = ctx.enter_context(nc.psum_tensor("ps", [P, 8, 512], F32))
        X_BANK = GATES * HALVES

        def bank(o, g):
            return GATES * o + g

        def slots(o, g):
            return ps[:, bank(o, g), 0:HC * SLOTS * B].rearrange("p (c s b) -> p c s b", c=HC, s=SLOTS)

        h_bf = h[:, :, :, :, :].bitcast(BF16)

        def h_half(part, s, o):
            return h[:, part, s, HC * o:HC * (o + 1), :]

        def h_half_top(part, s, o):
            return h_bf[:, part, s, HC * o:HC * (o + 1), 1::2]

        def cb(ap):
            return ap.rearrange("p (c b) -> p c b", c=HC)

        bias_loaded = sem("bias_loaded")
        h0_loaded = sem("h0_loaded")
        wh_loaded = [sem(f"wh_loaded{k}") for k in range(KC)]
        wx_loaded = sem("wx_loaded")
        x_loaded = sem("x_loaded")
        y_stored = sem("y_stored")
        first_cut = [sem(f"first_cut{k}") for k in range(KC)]
        next_cut = [sem(f"next_cut{k}") for k in range(KC)]
        rest_left = [sem(f"rest_left{k}") for k in range(KC)]
        start_rest = sem("start_rest")
        product = [[sem(f"product{o}{g}") for g in range(GATES)] for o in range(HALVES)]
        x_product = sem("x_product")
        pre_ready = [[sem(f"pre_ready{o}{g}") for g in (R, Z)] for o in range(HALVES)]
        m_scaled = halves("m_scaled")
        m_pre_ready = halves("m_pre_ready")
        zn_ready = halves("zn_ready")
        h_written = halves("h_written")
        rest1_written = halves("rest1_written")
        h_ready = halves("h_ready")
        r_ready = halves("r_ready")
        z_ready = halves("z_ready")
        omz_ready = halves("omz_ready")
        tanh_ready = halves("tanh_ready")
        refilled = halves("refilled")
        cm_placed = sem("cm_placed")
        xg_ready = sem("xg_ready")
        xg_0_ready = sem("xg_0_ready")
        x_padded = sem("x_padded")
        zh_ready = halves("zh_ready")
        xm_placed = halves("xm_placed")
        y_early = sem("y_early")
        y_late = sem("y_late")

        block = ctx.enter_context(nc.Block())

        def held(eng, value):
            return value if isinstance(value, int) else eng.snap(value)

        @block.sync
        def _(sp):
            sp.sem_inc(y_stored, 16)
            sp.dma_start(h[:, 0, STEPS - 1, :, :], h0).then_inc(h0_loaded, 16)
            sp.dma_start(bias_x[:, 0:2 * KC], w_b).then_inc(bias_loaded, 16)
            sp.dma_start(bias_x[:, 2 * KC:3 * KC], wx_b).then_inc(bias_loaded, 16)
            sp.dma_start(bias_h[:, :], wh_b).then_inc(bias_loaded, 16)
            x_flat = x.rearrange("p c t b -> p c (t b)")
            out_flat = out.rearrange("p c t b -> p c (t b)")
            for i in range(2):
                sp.dma_start(x_sb[:, :, i * TOK:(i + 1) * TOK], x_flat[:, :, i * TOK:(i + 1) * TOK])\
                    .then_inc(x_loaded, 16)

            def load_wh(k):
                sp.dma_start(wh_rest[:, k, 0:2 * D], w_W[D + k * P:D + (k + 1) * P, :]).then_inc(wh_loaded[k], 16)
                sp.dma_start(wh_rest[:, k, 2 * D:N], wh_W[k * P:(k + 1) * P, :]).then_inc(wh_loaded[k], 16)

            for k in range(KC // 2):
                load_wh(k)
            for k in range(KC):
                sp.dma_start(wx[:, k, 0:2 * D], w_W[k * P:(k + 1) * P, :]).then_inc(wx_loaded, 16)
                sp.dma_start(wx[:, k, 2 * D:N], wx_W[k * P:(k + 1) * P, :]).then_inc(wx_loaded, 16)
            for k in range(KC // 2, KC):
                load_wh(k)
            with sp.Fori(2, BLOCKS) as i:
                sp.wait_ge(x_loaded, sp.snap(i * 16))
                cols = bass.ds(sp.snap(i * TOK), TOK)
                sp.dma_start(x_sb[:, :, cols], x_flat[:, :, cols]).then_inc(x_loaded, 16)
            sp.wait_ge(x_loaded, BLOCKS * 16)
            sp.sem_inc(x_loaded, 16)
            with sp.Fori(0, BLOCKS) as i:
                done = sp.snap(i + 2)
                sp.wait_ge(y_early, done)
                sp.wait_ge(y_late, done)
                sp.dma_start(out_flat[:, :, bass.ds(sp.snap(i * TOK), TOK)],
                             y[:, :, :, :].rearrange("p c t b -> p c (t b)")).then_inc(y_stored, 16)
            sp.wait_ge(y_stored, 16 * (BLOCKS + 1))

        @block.tensor
        def _(pe):
            def x_products(plan, i_next, unit0):
                for u, k in plan:
                    g, c = divmod(u, KC)
                    if k == 0 and not (isinstance(unit0, int) and unit0 + u < 2):
                        pe.wait_ge(xg_ready, unit0 + (u - 1))
                    first = isinstance(i_next, int)
                    cols = slice(0, B + TOK) if first else bass.ds(i_next * TOK + B, TOK)
                    mm = pe.matmul(ps[:, X_BANK + u % 2, 0 if first else B:B + TOK],
                                   wx[:, k, g * D + c * P:g * D + (c + 1) * P], x_sb[:, k, cols],
                                   start=(k == 0), stop=(k == KC - 1))
                    if k == KC - 1:
                        mm.then_inc(x_product, 1)

            def products(o, g, chunks, ks, s):
                for ci in chunks:
                    col = g * D + (HC * o + ci) * P
                    for k in ks:
                        for part in range(PARTS):
                            mm = pe.matmul(ps[:, bank(o, g), ci * SLOTS * B:(ci * SLOTS + PARTS) * B],
                                           wh[:, part, k, col:col + P], h_bf[:, :, s - 1 if s else STEPS - 1, k, 1::2],
                                           start=(ci == 0 and k == 0 and part == 0),
                                           stop=(ci == HC - 1 and k == KC - 1 and part == PARTS - 1),
                                           skip_group_check=True)
                return mm

            ALL, FIRST, SECOND = range(HC), range(HC), range(HC, KC)

            def step(t0, s):
                nxt = held(pe, t0 + (s + 1))
                pe.wait_ge(h_ready[0], nxt)
                pe.wait_ge(refilled[0], nxt)
                products(0, R, ALL, FIRST, s)
                products(0, Z, ALL, FIRST, s)
                products(0, M, ALL, FIRST, s)
                pe.wait_ge(refilled[1], nxt)
                products(1, R, ALL, FIRST, s)
                products(1, Z, range(1), FIRST, s)
                pe.wait_ge(h_ready[1], nxt)
                for g in range(GATES):
                    products(0, g, ALL, SECOND, s).then_inc(product[0][g], 1)
                products(1, Z, range(1, HC), FIRST, s)
                products(1, M, ALL, FIRST, s)
                for g in range(GATES):
                    products(1, g, ALL, SECOND, s).then_inc(product[1][g], 1)

            pe.wait_ge(x_loaded, 2 * 16)
            pe.wait_ge(x_padded, 1)
            pe.wait_ge(wx_loaded, 2 * KC * 16)
            x_products(x_list, 0, 0)
            for k in range(KC):
                pe.wait_ge(first_cut[k], 1)
                pe.wait_ge(next_cut[k], PARTS - 1)
            pe.wait_ge(cm_placed, 1)
            with nc.Fori(0, BLOCKS - 1, engines=(mybir.EngineType.PE,), hint_back_edge=True) as i:
                t0 = pe.snap(i * STEPS)
                nxt_block = pe.snap(i + 1)
                unit0 = pe.snap(i * UNITS + UNITS)
                pe.wait_ge(x_loaded, pe.snap(t0 + 3 * 16))
                for s in range(STEPS):
                    step(t0, s)
                    x_products(X_PLAN[s], nxt_block, unit0)
            for s in range(STEPS):
                step(STEPS * (BLOCKS - 1), s)

        @block.scalar
        def _(act):
            def refill(o, addends):
                src = addends[:, :, R:Z + 1, o, :].rearrange("p a g (c b) -> p (a g) c b", c=HC)
                dst = ps[:, bank(o, R):bank(o, Z) + 1, 0:HC * SLOTS * B] \
                    .rearrange("p g (c s b) -> p g c s b", c=HC, s=SLOTS)[:, :, :, PARTS, :]
                act.activation(dst, src, ACT.Copy).then_inc(refilled[o], 1)

            def empty_0(u):
                g, c = divmod(u, KC)
                o, ci = divmod(c, HC)
                act.wait_ge(x_product, u + 1)
                act.activation(xg_0[:, 0, 0, g, o, ci * B:(ci + 1) * B], ps[:, X_BANK + u % 2, 0:B],
                               ACT.Identity, bias=bias_x[:, u:u + 1]).then_inc(xg_0_ready, 1)

            def empty(u, which, unit0):
                g, c = divmod(u, KC)
                o, ci = divmod(c, HC)
                act.wait_ge(x_product, unit0 + (u + 1))
                act.wait_ge(bias_loaded, 3 * 16)
                dst = xg[:, which, :, g, o, ci * B:(ci + 1) * B].rearrange("p a t b -> p (a t) b")
                act.activation(dst, ps[:, X_BANK + u % 2, B:B + TOK].rearrange("p (t b) -> p t b", b=B),
                               ACT.Identity, bias=bias_x[:, u:u + 1]).then_inc(xg_ready, 1)

            def step(t0, s, this, other, unit0, last):
                nxt = held(act, t0 + (s + 1))
                if s == 0:
                    empty(UNITS - 1, this, unit0 - UNITS)
                elif not last:
                    for u in X_ENDS[s - 1]:
                        empty(u, other, unit0)
                for o in range(HALVES):
                    act.wait_ge(pre_ready[o][R], nxt)
                    act.activation(r_gate[:, o, :], pre[:, o, R, :], ACT.Sigmoid).then_inc(r_ready[o], 1)
                    act.wait_ge(pre_ready[o][Z], nxt)
                    act.activation(z_gate[:, o, :], pre[:, o, Z, :], ACT.Sigmoid).then_inc(z_ready[o], 1)
                    act.activation(one_minus_z[:, o, :], pre[:, o, Z, :], ACT.Sigmoid, scale=-1.0)\
                        .then_inc(omz_ready[o], 1)
                    if s == 0 and o == 0:
                        act.wait_ge(xg_ready, unit0)
                    act.wait_ge(m_pre_ready[o], nxt)
                    act.activation(n_tanh[:, o, :], m_pre[:, o, :], ACT.Tanh).then_inc(tanh_ready[o], 1)
                    if not (last and s == STEPS - 1):
                        refill(o, xg[:, this, s])

            act.wait_ge(bias_loaded, 3 * 16)
            act.activation(n_tanh[:, 0, 0:KC], bias_h[:, :], ACT.Sigmoid)
            for o in range(HALVES):
                cm = bias_h[:, HC * o:HC * (o + 1)].unsqueeze(2).to_broadcast([P, HC, B])
                last_cm = act.activation(slots(o, M)[:, :, PARTS, :], cm, ACT.Copy)
            last_cm.then_inc(cm_placed, 1)

            def cut_part(part, k):
                act.wait_ge(rest_left[k], part)
                act.activation(wh[:, part, k, :], wh_rest[:, k, :], ACT.Copy).then_inc(next_cut[k], 1)

            for part, k in ((1, 0), (1, 1), (2, 0), (2, 1)):
                cut_part(part, k)
            cuts = {5: [(1, 2)], 8: [(1, 3), (2, 2)], 10: [(2, 3)]}
            for u in range(UNITS):
                empty_0(u)
                if u < UNITS - 1:
                    empty(u, slice(0, 1), 0)
                for part, k in cuts.get(u, []):
                    cut_part(part, k)
            act.wait_ge(xg_0_ready, UNITS)
            for o in range(HALVES):
                refill(o, xg_0[:, :, 0])
            with act.Fori(0, BLOCKS - 1) as i:
                t0 = act.snap(i * STEPS)
                this = bass.ds(act.snap(i % 2), 1)
                other = bass.ds(act.snap((i + 1) % 2), 1)
                unit0 = act.snap(i * UNITS + UNITS)
                for s in range(STEPS):
                    step(t0, s, this, other, unit0, False)
            final = slice((BLOCKS - 1) % 2, (BLOCKS - 1) % 2 + 1)
            for s in range(STEPS):
                step(STEPS * (BLOCKS - 1), s, final, None, UNITS * BLOCKS, True)

        @block.vector
        def _(dve):
            def gate_sum(o, g, nxt):
                dve.wait_ge(product[o][g], nxt)
                dve.tensor_reduce(cb(pre[:, o, g, :]), slots(o, g).rearrange("p c s b -> p c b s"),
                                  AX.X, ALU.add).then_inc(pre_ready[o][g], 1)

            def m_scale(o, nxt):
                dve.wait_ge(product[o][M], nxt)
                dve.wait_ge(r_ready[o], nxt)
                r = cb(r_gate[:, o, :]).unsqueeze(2).to_broadcast([P, HC, SLOTS, B])
                dve.tensor_tensor(m_terms[:, o, :, 0:SLOTS, :], slots(o, M), r, ALU.mult).then_inc(m_scaled[o], 1)

            def m_sum(o, nxt):
                dve.wait_ge(m_scaled[o], nxt)
                dve.wait_ge(xm_placed[o], nxt)
                dve.tensor_reduce(cb(m_pre[:, o, :]), m_terms[:, o, :, :, :].rearrange("p c s b -> p c b s"),
                                  AX.X, ALU.add).then_inc(m_pre_ready[o], 1)

            def scale_n(o, nxt):
                dve.wait_ge(omz_ready[o], nxt)
                dve.wait_ge(tanh_ready[o], nxt)
                dve.tensor_tensor(zn[:, o, :], one_minus_z[:, o, :], n_tanh[:, o, :], ALU.mult)\
                    .then_inc(zn_ready[o], 1)

            def write_h(o, s, nxt):
                dve.wait_ge(zn_ready[o], nxt)
                dve.wait_ge(zh_ready[o], nxt)
                dve.tensor_tensor(h_half(0, s, o), cb(zn[:, o, :]), cb(zh[:, o, :]), ALU.add)\
                    .then_inc(h_written[o], 1)

            def write_rest1(o, s, nxt):
                dve.wait_ge(h_written[o], nxt)
                dve.tensor_tensor(h_half(1, s, o), h_half(0, s, o), h_half_top(0, s, o), ALU.subtract)\
                    .then_inc(rest1_written[o], 1)

            def write_rest2(o, s, nxt):
                dve.wait_ge(rest1_written[o], nxt)
                dve.tensor_tensor(h_half(2, s, o), h_half(1, s, o), h_half_top(1, s, o), ALU.subtract)\
                    .then_inc(h_ready[o], 1)

            def step(t0, i, s):
                nxt = held(dve, t0 + (s + 1))
                if s == 0:
                    dve.wait_ge(y_early, held(dve, i + 1))
                if s == Y_HALF:
                    dve.wait_ge(y_late, held(dve, i + 1))
                gate_sum(0, R, nxt)
                gate_sum(0, Z, nxt)
                m_scale(0, nxt)
                m_sum(0, nxt)
                gate_sum(1, R, nxt)
                scale_n(0, nxt)
                write_h(0, s, nxt)
                gate_sum(1, Z, nxt)
                write_rest1(0, s, nxt)
                m_scale(1, nxt)
                write_rest2(0, s, nxt)
                m_sum(1, nxt)
                scale_n(1, nxt)
                write_h(1, s, nxt)
                write_rest1(1, s, nxt)
                write_rest2(1, s, nxt)

            S = STEPS - 1
            dve.wait_ge(h0_loaded, 16)
            for o in range(HALVES):
                dve.tensor_tensor(h_half(1, S, o), h_half(0, S, o), h_half_top(0, S, o), ALU.subtract)\
                    .then_inc(start_rest, 1)
            for o in range(HALVES):
                dve.wait_ge(start_rest, o + 1)
                dve.tensor_tensor(h_half(2, S, o), h_half(1, S, o), h_half_top(1, S, o), ALU.subtract)\
                    .then_inc(h_ready[o], 1)
            def take_off(part, k):
                dve.tensor_tensor(wh_rest[:, k, :], wh_rest[:, k, :], wh[:, part, k, :], ALU.subtract)\
                    .then_inc(rest_left[k], 1)

            for k in range(KC):
                dve.wait_ge(wh_loaded[k], 2 * 16)
                dve.tensor_copy(wh[:, 0, k, :], wh_rest[:, k, :]).then_inc(first_cut[k], 1)
                dve.wait_ge(first_cut[k], 1)
                take_off(0, k)
                if k % 2:
                    for k1 in (k - 1, k):
                        dve.wait_ge(next_cut[k1], 1)
                        take_off(1, k1)
            with dve.Fori(0, BLOCKS - 1) as i:
                t0 = dve.snap(i * STEPS)
                for s in range(STEPS):
                    step(t0, i, s)
            for s in range(STEPS):
                step(STEPS * (BLOCKS - 1), BLOCKS - 1, s)

        @block.gpsimd
        def _(pool):
            def place_xm(o, addends):
                pool.tensor_copy(m_terms[:, o, :, SLOTS, :],
                                 addends[:, :, M, o, :].rearrange("p a (c b) -> p (a c) b", c=HC))\
                    .then_inc(xm_placed[o], 1)

            def add_x(s0, base, early_or_late):
                cols = base + s0 * B
                xs = x_sb[:, :, cols:cols + Y_HALF * B] if isinstance(cols, int) else \
                    x_sb[:, :, bass.ds(cols, Y_HALF * B)]
                pool.tensor_tensor(y[:, :, s0:s0 + Y_HALF, :],
                                   xs.rearrange("p c (t b) -> p c t b", b=B),
                                   h[:, 0, s0:s0 + Y_HALF, :, :].rearrange("p t c b -> p c t b"), ALU.add)\
                    .then_inc(early_or_late, 1)

            def step(t0, s, this, unit0, last):
                nxt = held(pool, t0 + (s + 1))
                for o in range(HALVES):
                    if s == 0 and o == 0:
                        pool.wait_ge(xg_ready, unit0)
                    pool.wait_ge(z_ready[o], nxt)
                    pool.tensor_tensor(cb(zh[:, o, :]), cb(z_gate[:, o, :]), h_half(0, s - 1 if s else STEPS - 1, o),
                                       ALU.mult).then_inc(zh_ready[o], 1)
                    if not (last and s == STEPS - 1):
                        pool.wait_ge(m_pre_ready[o], nxt)
                        pool.wait_ge(xg_0_ready, UNITS)
                        place_xm(o, xg[:, this, s])
                if s % Y_HALF == Y_HALF - 1:
                    pool.wait_ge(h_written[0], nxt)
                    pool.wait_ge(h_written[1], nxt)
                    if s == Y_HALF - 1:
                        pool.wait_ge(y_stored, held(pool, t0 + 16))
                    pool.wait_ge(x_loaded, 16)
                    add_x(s + 1 - Y_HALF, t0 * B, y_early if s < Y_HALF else y_late)

            pool.memset(x_sb[:, :, T * B:T * B + B], 0.0).then_inc(x_padded, 1)
            pool.sem_inc(y_early, 1)
            pool.sem_inc(y_late, 1)
            pool.wait_ge(xg_0_ready, UNITS)
            for o in range(HALVES):
                place_xm(o, xg_0[:, :, 0])
            with pool.Fori(0, BLOCKS - 1) as i:
                t0 = pool.snap(i * STEPS)
                this = bass.ds(pool.snap(i % 2), 1)
                unit0 = pool.snap(i * UNITS + UNITS)
                for s in range(STEPS):
                    step(t0, s, this, unit0, False)
            final = slice((BLOCKS - 1) % 2, (BLOCKS - 1) % 2 + 1)
            for s in range(STEPS):
                step(STEPS * (BLOCKS - 1), s, final, UNITS * BLOCKS, True)


def kernel(x, cond_1024, L0_cond_w_W, L0_cond_w_b, L0_cond_wx_W, L0_cond_wx_b, L0_cond_wh_W, L0_cond_wh_b):
    import numpy as np
    import concourse.bacc as bacc
    from concourse.bass_utils import run_bass_kernel_spmd

    x, cond = np.asarray(x), np.asarray(cond_1024)
    B, T, D = x.shape
    KC = D // P

    def columns(v):
        return np.ascontiguousarray(np.asarray(v).reshape(-1, P).transpose(1, 0))

    arrays = {
        "x": np.ascontiguousarray(x.reshape(B, T, KC, P).transpose(3, 2, 1, 0)),
        "h0": np.ascontiguousarray(cond.reshape(B, KC, P).transpose(2, 1, 0)),
        "w_W": np.ascontiguousarray(L0_cond_w_W),
        "w_b": columns(L0_cond_w_b),
        "wx_W": np.ascontiguousarray(L0_cond_wx_W),
        "wx_b": columns(L0_cond_wx_b),
        "wh_W": np.ascontiguousarray(L0_cond_wh_W),
        "wh_b": columns(L0_cond_wh_b),
    }
    nc = bacc.Bacc("TRN2", target_bir_lowering=False, num_devices=1)
    args = {n: nc.dram_tensor(f"in_{n}", a.shape, F32, kind="ExternalInput").ap() for n, a in arrays.items()}
    out = nc.dram_tensor("out_h", (P, KC, T, B), F32, kind="ExternalOutput").ap()
    build(nc, out=out, **args)
    r = run_bass_kernel_spmd(nc, [{f"in_{n}": a for n, a in arrays.items()}], core_ids=[0])
    got = r.results[0]["out_h"]
    return np.ascontiguousarray(got.transpose(3, 2, 1, 0).reshape(B, T, D))
```
